# Optimizing a Trainium2 kernel written in Bass

```python
import numpy as np
import jax
import jax.numpy as jnp

def _softmax(x, axis=-1):
    return jax.nn.softmax(x, axis=axis)

def _gelu(x):
    return jax.nn.gelu(x, approximate=True)

def _silu(x):
    return jax.nn.silu(x)

def _sigmoid(x):
    return jax.nn.sigmoid(x)

def _layernorm(x, axis=-1, eps=1e-05):
    m = jnp.mean(x, axis=axis, keepdims=True)
    v = jnp.var(x, axis=axis, keepdims=True)
    return (x - m) / jnp.sqrt(v + eps)

def _scatter_add(tgt, idx, src, axis=0):
    return tgt.at[idx].add(src)

def _segment_sum(src, seg, n):
    return jax.ops.segment_sum(src, seg, n)
kernel_name = 'mk_dlrm_tower_d1_rec_r8_167dae'

def setup_inputs(seed: int=0):
    np.random.seed(seed)
    _w = jnp.asarray

    def _rec_inputs():
        import jax
        import jax.numpy as jnp
        _tk = jax.random.key(seed)
        ids = jnp.stack([jax.random.randint(jax.random.fold_in(_tk, 200 + f), (512,), 0, v, jnp.int32) for f, v in enumerate([1000, 1000, 125000, 1000, 12500, 12500, 1000, 1250, 1000, 12500, 12500, 1000, 1000, 1250, 1000, 1000, 1000, 12500, 1000, 12500, 1000, 1250, 1250, 1250, 12500, 1250])], axis=1)
        tbl_0 = 0.05 * jax.random.normal(jax.random.fold_in(_tk, 500 + 0), (1000, 128), jnp.float32)
        tbl_1 = 0.05 * jax.random.normal(jax.random.fold_in(_tk, 500 + 1), (1000, 128), jnp.float32)
        tbl_2 = 0.05 * jax.random.normal(jax.random.fold_in(_tk, 500 + 2), (125000, 128), jnp.float32)
        tbl_3 = 0.05 * jax.random.normal(jax.random.fold_in(_tk, 500 + 3), (1000, 128), jnp.float32)
        tbl_4 = 0.05 * jax.random.normal(jax.random.fold_in(_tk, 500 + 4), (12500, 128), jnp.float32)
        tbl_5 = 0.05 * jax.random.normal(jax.random.fold_in(_tk, 500 + 5), (12500, 128), jnp.float32)
        tbl_6 = 0.05 * jax.random.normal(jax.random.fold_in(_tk, 500 + 6), (1000, 128), jnp.float32)
        tbl_7 = 0.05 * jax.random.normal(jax.random.fold_in(_tk, 500 + 7), (1250, 128), jnp.float32)
        tbl_8 = 0.05 * jax.random.normal(jax.random.fold_in(_tk, 500 + 8), (1000, 128), jnp.float32)
        tbl_9 = 0.05 * jax.random.normal(jax.random.fold_in(_tk, 500 + 9), (12500, 128), jnp.float32)
        tbl_10 = 0.05 * jax.random.normal(jax.random.fold_in(_tk, 500 + 10), (12500, 128), jnp.float32)
        tbl_11 = 0.05 * jax.random.normal(jax.random.fold_in(_tk, 500 + 11), (1000, 128), jnp.float32)
        tbl_12 = 0.05 * jax.random.normal(jax.random.fold_in(_tk, 500 + 12), (1000, 128), jnp.float32)
        tbl_13 = 0.05 * jax.random.normal(jax.random.fold_in(_tk, 500 + 13), (1250, 128), jnp.float32)
        tbl_14 = 0.05 * jax.random.normal(jax.random.fold_in(_tk, 500 + 14), (1000, 128), jnp.float32)
        tbl_15 = 0.05 * jax.random.normal(jax.random.fold_in(_tk, 500 + 15), (1000, 128), jnp.float32)
        tbl_16 = 0.05 * jax.random.normal(jax.random.fold_in(_tk, 500 + 16), (1000, 128), jnp.float32)
        tbl_17 = 0.05 * jax.random.normal(jax.random.fold_in(_tk, 500 + 17), (12500, 128), jnp.float32)
        tbl_18 = 0.05 * jax.random.normal(jax.random.fold_in(_tk, 500 + 18), (1000, 128), jnp.float32)
        tbl_19 = 0.05 * jax.random.normal(jax.random.fold_in(_tk, 500 + 19), (12500, 128), jnp.float32)
        tbl_20 = 0.05 * jax.random.normal(jax.random.fold_in(_tk, 500 + 20), (1000, 128), jnp.float32)
        tbl_21 = 0.05 * jax.random.normal(jax.random.fold_in(_tk, 500 + 21), (1250, 128), jnp.float32)
        tbl_22 = 0.05 * jax.random.normal(jax.random.fold_in(_tk, 500 + 22), (1250, 128), jnp.float32)
        tbl_23 = 0.05 * jax.random.normal(jax.random.fold_in(_tk, 500 + 23), (1250, 128), jnp.float32)
        tbl_24 = 0.05 * jax.random.normal(jax.random.fold_in(_tk, 500 + 24), (12500, 128), jnp.float32)
        tbl_25 = 0.05 * jax.random.normal(jax.random.fold_in(_tk, 500 + 25), (1250, 128), jnp.float32)
        _rk = jax.random.fold_in(_tk, 7)
        r_dense_features = -0.000520686 + 1.00062 * jax.random.normal(jax.random.fold_in(_rk, 101), (512, 128), jnp.float32)
        W_top1 = 0.0405887 * jax.random.normal(jax.random.fold_in(_tk, 801), (607, 512), jnp.float32)
        W_top2 = 0.0441942 * jax.random.normal(jax.random.fold_in(_tk, 802), (512, 256), jnp.float32)
        W_top3 = 0.0625 * jax.random.normal(jax.random.fold_in(_tk, 803), (256, 1), jnp.float32)
        b_top1 = jnp.zeros((512,), jnp.float32)
        b_top2 = jnp.zeros((256,), jnp.float32)
        return (r_dense_features, ids, tbl_0, tbl_1, tbl_2, tbl_3, tbl_4, tbl_5, tbl_6, tbl_7, tbl_8, tbl_9, tbl_10, tbl_11, tbl_12, tbl_13, tbl_14, tbl_15, tbl_16, tbl_17, tbl_18, tbl_19, tbl_20, tbl_21, tbl_22, tbl_23, tbl_24, tbl_25, W_top1, b_top1, W_top2, b_top2, W_top3)
    r_dense_features, ids, tbl_0, tbl_1, tbl_2, tbl_3, tbl_4, tbl_5, tbl_6, tbl_7, tbl_8, tbl_9, tbl_10, tbl_11, tbl_12, tbl_13, tbl_14, tbl_15, tbl_16, tbl_17, tbl_18, tbl_19, tbl_20, tbl_21, tbl_22, tbl_23, tbl_24, tbl_25, W_top1, b_top1, W_top2, b_top2, W_top3 = _rec_inputs()

    def _L0_rec_setup():
        import jax, jax.numpy as jnp
        import numpy as np
        NUM_SPARSE = 26
        EMBED_DIM = 128
        BATCH = 2048
        key = jax.random.key(seed)
        k1, k2 = jax.random.split(key)
        dense_features = jax.random.normal(k1, (BATCH, EMBED_DIM), dtype=jnp.float32)
        sparse_features = jax.random.normal(k2, (BATCH, NUM_SPARSE, EMBED_DIM), dtype=jnp.float32)
        return {'dense_features': dense_features, 'sparse_features': sparse_features}
    _L0_rec_all = _L0_rec_setup()
    _L0_rec_in = {k: v for k, v in _L0_rec_all.items() if k in ()}
    del _L0_rec_all
    return {'r_dense_features': r_dense_features, 'ids': ids, 'tbl_0': tbl_0, 'tbl_1': tbl_1, 'tbl_2': tbl_2, 'tbl_3': tbl_3, 'tbl_4': tbl_4, 'tbl_5': tbl_5, 'tbl_6': tbl_6, 'tbl_7': tbl_7, 'tbl_8': tbl_8, 'tbl_9': tbl_9, 'tbl_10': tbl_10, 'tbl_11': tbl_11, 'tbl_12': tbl_12, 'tbl_13': tbl_13, 'tbl_14': tbl_14, 'tbl_15': tbl_15, 'tbl_16': tbl_16, 'tbl_17': tbl_17, 'tbl_18': tbl_18, 'tbl_19': tbl_19, 'tbl_20': tbl_20, 'tbl_21': tbl_21, 'tbl_22': tbl_22, 'tbl_23': tbl_23, 'tbl_24': tbl_24, 'tbl_25': tbl_25, 'W_top1': W_top1, 'b_top1': b_top1, 'W_top2': W_top2, 'b_top2': b_top2, 'W_top3': W_top3}

def reference(r_dense_features, ids, tbl_0, tbl_1, tbl_2, tbl_3, tbl_4, tbl_5, tbl_6, tbl_7, tbl_8, tbl_9, tbl_10, tbl_11, tbl_12, tbl_13, tbl_14, tbl_15, tbl_16, tbl_17, tbl_18, tbl_19, tbl_20, tbl_21, tbl_22, tbl_23, tbl_24, tbl_25, W_top1, b_top1, W_top2, b_top2, W_top3):
    import jax
    import jax.numpy as jnp

    def _L0_rec_ref(dense_features, sparse_features):
        import jax, jax.numpy as jnp
        import numpy as np
        NUM_SPARSE = 26
        EMBED_DIM = 128
        BATCH = 2048
        F = NUM_SPARSE + 1
        combined = jnp.concatenate([dense_features[:, None, :], sparse_features], axis=1)
        interactions = jnp.einsum('bfd,bgd->bfg', combined, combined)
        iu, ju = jnp.triu_indices(F, k=1)
        interactions_flat = interactions[:, iu, ju]
        return jnp.concatenate([dense_features, interactions_flat], axis=1)
    e = jnp.stack([tbl_0[ids[:, 0]], tbl_1[ids[:, 1]], tbl_2[ids[:, 2]], tbl_3[ids[:, 3]], tbl_4[ids[:, 4]], tbl_5[ids[:, 5]], tbl_6[ids[:, 6]], tbl_7[ids[:, 7]], tbl_8[ids[:, 8]], tbl_9[ids[:, 9]], tbl_10[ids[:, 10]], tbl_11[ids[:, 11]], tbl_12[ids[:, 12]], tbl_13[ids[:, 13]], tbl_14[ids[:, 14]], tbl_15[ids[:, 15]], tbl_16[ids[:, 16]], tbl_17[ids[:, 17]], tbl_18[ids[:, 18]], tbl_19[ids[:, 19]], tbl_20[ids[:, 20]], tbl_21[ids[:, 21]], tbl_22[ids[:, 22]], tbl_23[ids[:, 23]], tbl_24[ids[:, 24]], tbl_25[ids[:, 25]]], axis=1)
    z = _L0_rec_ref(r_dense_features, e)
    z = z.reshape(z.shape[0], -1)
    h = jnp.concatenate([z, r_dense_features], axis=1)
    h = jnp.maximum(h @ W_top1 + b_top1, 0.0)
    h = jnp.maximum(h @ W_top2 + b_top2, 0.0)
    y = h @ W_top3
    return y

_drawn_inputs = setup_inputs


def setup_inputs(seed=0):
    import zlib

    import numpy as np

    out = dict(_drawn_inputs(seed))
    spreads = {'b_top1': (0.0, 0.1), 'b_top2': (0.0, 0.1)}
    factors = {}
    for name, (base, spread) in spreads.items():
        noise = np.random.default_rng([zlib.crc32(name.encode()), seed]).standard_normal(out[name].shape)
        drawn = base * np.exp(spread * noise) if base else spread * noise
        out[name] = jnp.asarray(drawn.astype(out[name].dtype))
    for name, factor in factors.items():
        out[name] = (out[name] * factor).astype(out[name].dtype)
    return out
```

```python
from contextlib import ExitStack

import numpy as np

import concourse.bass as bass
from concourse import mybir

P = 128
QUAD = 32
BATCH, DIM, SPARSE = 512, 128, 26
FEATS = SPARSE + 1
TILES = BATCH // P
SLOTS = P // 4
HID1, HID2 = 512, 256
N1, N2 = HID1 // P, HID2 // P
COLS = FEATS - 1
CHUNKS = -(-COLS // 4)
BANK = 512
SLOTS_PER_BANK = 16
GROUP = 4

FIELD_AT = list(range(FEATS))
GATHERED = list(range(1, FEATS))
GROUPS = [GATHERED[i:i + GROUP] for i in range(0, len(GATHERED), GROUP)]


def chunk_rows(c):
    return QUAD * (min(4, COLS - 4 * c) - 1) + FEATS


def tower(nc, dense, ids, tables, w_inter, w_dense, b1, w2, b2, w3, out):
    fp32, i32 = mybir.dt.float32, mybir.dt.int32
    ALU, ACT = mybir.AluOpType, mybir.ActivationFunctionType

    with ExitStack() as ctx:
        def sb(name, shape, dt=fp32):
            return ctx.enter_context(nc.sbuf_tensor(name, shape, dt))

        def pb(name, cols):
            return ctx.enter_context(nc.psum_tensor(name, [P, cols], fp32))

        def sem(name):
            return ctx.enter_context(nc.semaphore(name))

        ids_sb = sb("ids_sb", [P, TILES * SPARSE], i32)
        dense_sb = sb("dense_sb", [P, TILES, DIM])
        gathered = sb("gathered", [P, TILES, len(GATHERED), DIM])
        featT = sb("featT", [P, BATCH, FEATS])
        denseT = sb("denseT", [P, BATCH])
        zT = sb("zT", [P, CHUNKS, BATCH])
        w_inter_sb = sb("w_inter_sb", [P, CHUNKS, HID1])
        w_dense_sb = sb("w_dense_sb", [P, 2, HID1])
        w_dsum = sb("w_dsum", [P, HID1])
        w2_sb = sb("w2_sb", [P, N1, HID2])
        w3_sb = sb("w3_sb", [P, N2])
        b1_sb = sb("b1_sb", [P, N1])
        b2_sb = sb("b2_sb", [P, N2])
        h1 = sb("h1", [P, N1, P])
        h2 = sb("h2", [P, N2, P])
        y_sb = sb("y_sb", [1, BATCH])
        ident = sb("ident", [P, P])

        fill_ps = [pb(f"fill_ps{i}", BANK) for i in range(2)]
        gram_ps = [pb(f"gram_ps{i}", 2 * BANK) for i in range(2)]
        h1_ps = pb("h1_ps", BANK)
        h2_ps = pb("h2_ps", BANK)

        ids_in = sem("ids_in")
        dense_in = sem("dense_in")
        w_inter_in = sem("w_inter_in")
        w_dense_in = sem("w_dense_in")
        w2_in = sem("w2_in")
        small_in = sem("small_in")
        rows_in = [[sem(f"rows_in{t}_{g}") for g in range(len(GROUPS))] for t in range(TILES)]
        ident_zero = sem("ident_zero")
        ident_ready = sem("ident_ready")
        zT_zeroed = sem("zT_zeroed")
        dsum_ready = sem("dsum_ready")
        filled = [sem(f"filled{i}") for i in range(2)]
        fill_read = [sem(f"fill_read{i}") for i in range(2)]
        gram_ready = sem("gram_ready")
        z_dve = sem("z_dve")
        z_act = sem("z_act")
        h1_psum = sem("h1_psum")
        h1_ready = sem("h1_ready")
        h2_psum = sem("h2_psum")
        h2_ready = sem("h2_ready")
        y_psum = sem("y_psum")
        y_ready = sem("y_ready")
        out_done = sem("out_done")

        block = ctx.enter_context(nc.Block())

        def fill_no(t, g):
            return 1 + t * len(GROUPS) + g

        def fills_of_bank(bank, upto):
            return (upto - bank + 1) // 2

        def group_source(bank, g):
            n = len(GROUPS[g])
            return fill_ps[bank][:, 0:n * P].rearrange("d (f b) -> d b f", f=n)

        def group_target(t, g):
            first = GROUPS[g][0]
            return featT[:, t * P:(t + 1) * P, first:first + len(GROUPS[g])]

        def z_source(t, j, q):
            view = gram_ps[t % 2][QUAD * j:QUAD * j + FEATS, :].rearrange("i (k w) -> i k w", k=2)
            view = view[:, :, 0:SLOTS_PER_BANK * COLS].rearrange("i k (s g) -> i k s g", g=COLS)
            return view[:, :, :, q:COLS:4].rearrange("i k s c -> i c k s")

        def z_target(t, j, q):
            n = len(range(q, COLS, 4))
            b0 = t * P + j * SLOTS
            return zT[QUAD * q:QUAD * q + FEATS, 0:n, b0:b0 + SLOTS].rearrange("i c (k s) -> i c k s", k=2)

        @block.sync
        def _(sp):
            sp.dma_start(ids_sb[:, :], ids).then_inc(ids_in, 16)
            sp.dma_start(dense_sb[:, :, :], dense.rearrange("(t p) d -> p t d", p=P)).then_inc(dense_in, 16)
            sp.dma_start(w_inter_sb[:, :, :], w_inter).then_inc(w_inter_in, 16)
            sp.wait_ge(y_ready, TILES)
            sp.dma_start(out.rearrange("b a -> a b"), y_sb[:, :]).then_inc(out_done, 16)
            sp.wait_ge(out_done, 16)

        @block.gpsimd
        def _(pool):
            pool.memset(ident[:, :], 0.0).then_inc(ident_zero, 1)
            pool.wait_ge(ident_zero, 1)
            pool.affine_select(out=ident[:, :], in_=ident[:, :], compare_op=ALU.not_equal, fill=1.0,
                               base=0, pattern=[[-1, P]], channel_multiplier=1).then_inc(ident_ready, 1)
            pool.wait_ge(ids_in, 16)
            for t in range(TILES):
                for g, group in enumerate(GROUPS):
                    for pos in group:
                        table = FIELD_AT[pos] - 1
                        col = t * SPARSE + table
                        pool.indirect_dma_start(
                            out=gathered[:, t, pos - 1, :], out_offset=None, in_=tables[table],
                            in_offset=bass.IndirectOffsetOnAxis(ap=ids_sb[:, col:col + 1], axis=0),
                        ).then_inc(rows_in[t][g], 16)

        @block.scalar
        def _(act):
            act.dma_start(w_dense_sb[:, :, :], w_dense).then_inc(w_dense_in, 16)
            act.dma_start(w2_sb[:, :, :], w2.rearrange("(k p) n -> p k n", p=P)).then_inc(w2_in, 16)
            act.dma_start(w3_sb[:, :], w3).then_inc(small_in, 16)
            act.dma_start(b1_sb[:, :], b1).then_inc(small_in, 16)
            act.dma_start(b2_sb[:, :], b2).then_inc(small_in, 16)

            def fill_to_featT(t, g):
                n = fill_no(t, g)
                if n % 2 == 1:
                    act.wait_ge(filled[1], n // 2 + 1)
                    nc.scalar.activation(group_target(t, g), group_source(1, g), ACT.Copy) \
                        .then_inc(fill_read[1], 1)

            def hidden2(t):
                act.wait_ge(h2_psum, t + 1)
                for n in range(N2):
                    nc.scalar.activation(h2[:, n, :], h2_ps[:, n * P:(n + 1) * P], ACT.Relu,
                                         bias=b2_sb[:, n:n + 1]).then_inc(h2_ready, 1)

            for t in range(TILES):
                for g in range(len(GROUPS)):
                    fill_to_featT(t, g)
                    if t == 1 and g == 1:
                        act.wait_ge(small_in, 48)
                    if t > 0 and g == 2:
                        hidden2(t - 1)
                act.wait_ge(gram_ready, t + 1)
                if t == 0:
                    act.wait_ge(zT_zeroed, 1)
                for j in (2, 3):
                    for q in range(4):
                        nc.scalar.activation(z_target(t, j, q), z_source(t, j, q), ACT.Copy) \
                            .then_inc(z_act, 1)
            hidden2(TILES - 1)

        @block.vector
        def _(dve):
            nc.vector.memset(zT[:, :, :], 0.0).then_inc(zT_zeroed, 1)
            dve.wait_ge(filled[0], 1)
            nc.vector.tensor_copy(denseT[:, :], fill_ps[0][:, :])
            nc.vector.tensor_copy(featT[:, :, 0], fill_ps[0][:, :]).then_inc(fill_read[0], 1)
            dve.wait_ge(w_dense_in, 16)
            nc.vector.tensor_tensor(w_dsum[:, :], w_dense_sb[:, 0, :], w_dense_sb[:, 1, :], ALU.add) \
                .then_inc(dsum_ready, 1)

            def fill_to_featT(t, g):
                n = fill_no(t, g)
                if n % 2 == 0:
                    dve.wait_ge(filled[0], n // 2 + 1)
                    nc.vector.tensor_copy(group_target(t, g), group_source(0, g)).then_inc(fill_read[0], 1)

            def hidden1(t):
                dve.wait_ge(h1_psum, t + 1)
                for n in range(N1):
                    nc.vector.tensor_scalar(h1[:, n, :], h1_ps[:, n * P:(n + 1) * P], b1_sb[:, n:n + 1], 0.0,
                                            ALU.add, ALU.max).then_inc(h1_ready, 1)

            def scores(t):
                dve.wait_ge(y_psum, t + 1)
                nc.vector.tensor_copy(y_sb[0:1, t * P:(t + 1) * P], h2_ps[0:1, N2 * P:(N2 + 1) * P]) \
                    .then_inc(y_ready, 1)

            for t in range(TILES):
                for g in range(len(GROUPS)):
                    fill_to_featT(t, g)
                    if t == 1 and g == 1:
                        dve.wait_ge(small_in, 48)
                    if t > 0 and g == 1:
                        hidden1(t - 1)
                    if t > 0 and g == 3:
                        scores(t - 1)
                dve.wait_ge(gram_ready, t + 1)
                if t == 0:
                    dve.wait_ge(zT_zeroed, 1)
                for j in (0, 1):
                    for q in range(4):
                        nc.vector.tensor_copy(z_target(t, j, q), z_source(t, j, q)).then_inc(z_dve, 1)
            hidden1(TILES - 1)
            scores(TILES - 1)

        @block.tensor
        def _(pe):
            pe.wait_ge(ident_ready, 1)
            pe.wait_ge(dense_in, 16)
            for t in range(TILES):
                last = nc.tensor.transpose(fill_ps[0][:, t * P:(t + 1) * P], dense_sb[:, t, :], ident[:, :])
            last.then_inc(filled[0], 1)

            def fill(t, g):
                n = fill_no(t, g)
                pe.wait_ge(rows_in[t][g], 16 * len(GROUPS[g]))
                if n >= 2:
                    pe.wait_ge(fill_read[n % 2], n // 2)
                for i, pos in enumerate(GROUPS[g]):
                    last = nc.tensor.transpose(fill_ps[n % 2][:, i * P:(i + 1) * P],
                                               gathered[:, t, pos - 1, :], ident[:, :])
                last.then_inc(filled[n % 2], 1)

            def gram(t):
                for bank in range(2):
                    pe.wait_ge(fill_read[bank], fills_of_bank(bank, fill_no(t + 1, 0)))
                if t >= 2:
                    pe.wait_ge(z_dve, 8 * (t - 1))
                    pe.wait_ge(z_act, 8 * (t - 1))
                for s in range(SLOTS):
                    col = BANK * (s // SLOTS_PER_BANK) + COLS * (s % SLOTS_PER_BANK)
                    for j in range(4):
                        b = t * P + j * SLOTS + s
                        last = nc.tensor.matmul(gram_ps[t % 2][QUAD * j:QUAD * j + FEATS, col:col + COLS],
                                                featT[:, b, :], featT[:, b, 1:FEATS], start=True, stop=True)
                last.then_inc(gram_ready, 1)

            def layer1(t):
                tile = slice(t * P, (t + 1) * P)
                if t == 0:
                    pe.wait_ge(dsum_ready, 1)
                    pe.wait_ge(w_inter_in, 16)
                pe.wait_ge(z_dve, 8 * (t + 1))
                pe.wait_ge(z_act, 8 * (t + 1))
                if t > 0:
                    pe.wait_ge(h1_ready, N1 * t)
                for n in range(N1):
                    units = slice(n * P, (n + 1) * P)
                    nc.tensor.matmul(h1_ps[:, units], w_dsum[:, units], denseT[:, tile], start=True, stop=False)
                    for c in range(CHUNKS):
                        k = chunk_rows(c)
                        last = nc.tensor.matmul(h1_ps[:, units], w_inter_sb[0:k, c, units], zT[0:k, c, tile],
                                                start=False, stop=(c == CHUNKS - 1))
                last.then_inc(h1_psum, 1)

            def layer2(t):
                if t == 0:
                    pe.wait_ge(w2_in, 16)
                pe.wait_ge(h1_ready, N1 * (t + 1))
                if t > 0:
                    pe.wait_ge(y_ready, t)
                for n in range(N2):
                    for k in range(N1):
                        last = nc.tensor.matmul(h2_ps[:, n * P:(n + 1) * P], w2_sb[:, k, n * P:(n + 1) * P],
                                                h1[:, k, :], start=(k == 0), stop=(k == N1 - 1))
                last.then_inc(h2_psum, 1)

            def layer3(t):
                if t == 0:
                    pe.wait_ge(small_in, 48)
                pe.wait_ge(h2_ready, N2 * (t + 1))
                for k in range(N2):
                    last = nc.tensor.matmul(h2_ps[0:1, N2 * P:(N2 + 1) * P], w3_sb[:, k:k + 1], h2[:, k, :],
                                            start=(k == 0), stop=(k == N2 - 1))
                last.then_inc(y_psum, 1)

            for t in range(TILES):
                for g in range(len(GROUPS)):
                    fill(t, g)
                    if t > 0 and g == 0:
                        layer1(t - 1)
                    if t > 0 and g == 1:
                        layer2(t - 1)
                    if t > 0 and g == 2:
                        layer3(t - 1)
                gram(t)
            layer1(TILES - 1)
            layer2(TILES - 1)
            layer3(TILES - 1)


def first_layer_layout(w1):
    w = np.zeros((P, CHUNKS, HID1), w1.dtype)
    for g in range(1, FEATS):
        c, q = divmod(g - 1, 4)
        for i in range(g):
            lo, hi = sorted((FIELD_AT[i], FIELD_AT[g]))
            pair = lo * FEATS - lo * (lo + 1) // 2 + (hi - lo - 1)
            w[QUAD * q + i, c] = w1[DIM + pair]
    return w


def kernel(**inputs):
    import numpy as _np
    import concourse.bacc as _bacc
    from concourse import mybir as _mybir
    from concourse.bass_utils import run_bass_kernel_spmd as _run

    arr = {k: _np.ascontiguousarray(v) for k, v in inputs.items()}
    w1 = arr["W_top1"]
    data = {
        "dense": arr["r_dense_features"],
        "ids": _np.ascontiguousarray(arr["ids"].reshape(TILES, P, SPARSE).transpose(1, 0, 2).reshape(P, -1)),
        **{f"tbl_{n}": arr[f"tbl_{n}"] for n in range(SPARSE)},
        "w_inter": first_layer_layout(w1),
        "w_dense": _np.ascontiguousarray(_np.stack([w1[:DIM], w1[-DIM:]], axis=1)),
        "b1": _np.ascontiguousarray(arr["b_top1"].reshape(N1, P).T),
        "w2": arr["W_top2"],
        "b2": _np.ascontiguousarray(arr["b_top2"].reshape(N2, P).T),
        "w3": _np.ascontiguousarray(arr["W_top3"].reshape(N2, P).T),
    }
    nc = _bacc.Bacc("TRN2", target_bir_lowering=False, num_devices=1)
    ap = {k: nc.dram_tensor(k, v.shape, _mybir.dt.from_np(v.dtype), kind="ExternalInput").ap()
          for k, v in data.items()}
    out = nc.dram_tensor("scores", (BATCH, 1), _mybir.dt.float32, kind="ExternalOutput").ap()
    tower(nc, ap["dense"], ap["ids"], [ap[f"tbl_{n}"] for n in range(SPARSE)], ap["w_inter"], ap["w_dense"],
          ap["b1"], ap["w2"], ap["b2"], ap["w3"], out)
    r = _run(nc, [data], core_ids=[0])
    return r.results[0]["scores"]
```

```python
from contextlib import ExitStack

import numpy as np

import concourse.bass as bass
from concourse import mybir

P = 128
QUAD = 32
BATCH, DIM, SPARSE = 512, 128, 26
FEATS = SPARSE + 1
TILES = BATCH // P
SLOTS = P // 4
HID1, HID2 = 512, 256
N1, N2 = HID1 // P, HID2 // P
COLS = FEATS - 1
CHUNKS = -(-COLS // 4)
BANK = 512
SLOTS_PER_BANK = 16
GROUP = 4

ONEHOT_TABLES = (0, 1, 3, 6, 8)
ONEHOTS = len(ONEHOT_TABLES)
ROWS = 1000
RCHUNKS = 8
RPARTS = ROWS // RCHUNKS
DVE_CHUNKS = 6
DVE_STEP = 3
FIELD_AT = [0] + [1 + n for n in ONEHOT_TABLES] + [1 + n for n in range(SPARSE) if n not in ONEHOT_TABLES]
GATHERED = list(range(1 + ONEHOTS, FEATS))
GROUPS = [[g for g in range(4 * c + 1, 4 * c + 5) if g in GATHERED] for c in range(CHUNKS)]
GROUPS = [group for group in GROUPS if group]
LAST = TILES - 1
STAGES = [(t, 0, CHUNKS) for t in range(LAST)] + [(LAST, 0, 4), (LAST, 4, CHUNKS - 1), (LAST, CHUNKS - 1, CHUNKS)]


L21_AFTER, L3_AFTER = 1, 3


def last_position(c1):
    return min(4 * c1, COLS)


def copies(stage):
    _, c0, c1 = STAGES[stage]
    return 2 * min(4, last_position(c1) - 4 * c0)


def copies_done(stage):
    return sum(copies(u) for u in range(stage + 1))


def groups_of_stage(stage):
    t, c0, c1 = STAGES[stage]
    return [g for g, group in enumerate(GROUPS) if 4 * c0 < group[-1] <= last_position(c1)]


def chunk_rows(c):
    return QUAD * (min(4, COLS - 4 * c) - 1) + FEATS - 1


def tower(nc, dense, ids, oh_ids, tables, w_inter, w_dense, b1, w2, b2, w3, out):
    fp32, fp32r, i32 = mybir.dt.float32, mybir.dt.float32r, mybir.dt.int32
    ALU, ACT = mybir.AluOpType, mybir.ActivationFunctionType

    with ExitStack() as ctx:
        def sb(name, shape, dt=fp32):
            return ctx.enter_context(nc.sbuf_tensor(name, shape, dt))

        def pb(name, cols):
            return ctx.enter_context(nc.psum_tensor(name, [P, cols], fp32))

        def sem(name):
            return ctx.enter_context(nc.semaphore(name))

        ids_sb = sb("ids_sb", [P, TILES * SPARSE], i32)
        oh_ids_sb = sb("oh_ids_sb", [RPARTS, ONEHOTS, BATCH], i32)
        rowno_i = sb("rowno_i", [RPARTS, RCHUNKS], i32)
        rowno = sb("rowno", [RPARTS, RCHUNKS])
        minus_rowno = sb("minus_rowno", [RPARTS, RCHUNKS])
        id_off = sb("id_off", [RPARTS, BATCH])
        table_sb = sb("table_sb", [RPARTS, 3, RCHUNKS * DIM])
        table_hi = sb("table_hi", [RPARTS, 2, RCHUNKS * DIM], fp32r)
        table_lo = sb("table_lo", [RPARTS, 2, RCHUNKS * DIM], fp32r)
        onehot = sb("onehot", [RPARTS, RCHUNKS, BATCH], fp32r)
        dense_sb = sb("dense_sb", [P, TILES, DIM])
        gathered = sb("gathered", [P, TILES, len(GATHERED), DIM])
        featT = sb("featT", [P, BATCH, FEATS])
        denseT = sb("denseT", [P, BATCH])
        zT = sb("zT", [P, CHUNKS, BATCH])
        w_inter_sb = sb("w_inter_sb", [P, CHUNKS, HID1])
        w_dense_sb = sb("w_dense_sb", [P, 2, HID1])
        w_dsum = sb("w_dsum", [P, HID1])
        w2_sb = sb("w2_sb", [P, N1, HID2])
        w3_sb = sb("w3_sb", [P, N2])
        b1_sb = sb("b1_sb", [P, N1])
        b2_sb = sb("b2_sb", [P, N2])
        h1 = sb("h1", [P, N1, P])
        h2 = sb("h2", [P, N2, P])
        y_sb = sb("y_sb", [1, BATCH])
        ident = sb("ident", [P, P])

        fill_ps = [pb(f"fill_ps{i}", BANK) for i in range(2)]
        gram_ps = [pb(f"gram_ps{i}", 2 * BANK) for i in range(2)]
        h1_ps = pb("h1_ps", BANK)
        h2_ps = pb("h2_ps", BANK)

        ids_in = sem("ids_in")
        dense_in = sem("dense_in")
        table_in = [sem(f"table_in{k}") for k in range(ONEHOTS)]
        oh_ids_in = [sem(f"oh_ids_in{i}") for i in range(2)]
        rowno_int = sem("rowno_int")
        rowno_ready = sem("rowno_ready")
        hi_ready = sem("hi_ready")
        lo_ready = sem("lo_ready")
        ids_psum = sem("ids_psum")
        onehot_dve = sem("onehot_dve")
        onehot_act = sem("onehot_act")
        id_off_ready = sem("id_off_ready")
        onehot_used = sem("onehot_used")
        w_inter_in = sem("w_inter_in")
        w_dense_in = sem("w_dense_in")
        w2_in = sem("w2_in")
        small_in = sem("small_in")
        rows_in = [[sem(f"rows_in{t}_{g}") for g in range(len(GROUPS))] for t in range(TILES)]
        ident_zero = sem("ident_zero")
        ident_ready = sem("ident_ready")
        zT_zeroed = sem("zT_zeroed")
        dsum_ready = sem("dsum_ready")
        filled = [sem(f"filled{i}") for i in range(2)]
        fill_read = [sem(f"fill_read{i}") for i in range(2)]
        gram_ready = sem("gram_ready")
        z_dve = sem("z_dve")
        z_act = sem("z_act")
        h1_psum = sem("h1_psum")
        h1_ready = sem("h1_ready")
        h2_psum = sem("h2_psum")
        h2_ready = sem("h2_ready")
        y_psum = sem("y_psum")
        y_ready = sem("y_ready")
        out_done = sem("out_done")

        block = ctx.enter_context(nc.Block())

        def fill_no(t, g):
            return 1 + ONEHOTS + t * len(GROUPS) + g

        def fills_of_bank(bank, upto):
            return (upto - bank + 1) // 2

        def transposed(n):
            return n // 2 + 1 - len([k for k in range(ONEHOTS) if (1 + k) % 2 == n % 2])

        def group_source(bank, g):
            n = len(GROUPS[g])
            return fill_ps[bank][:, 0:n * P].rearrange("d (f b) -> d b f", f=n)

        def group_target(t, g):
            first = GROUPS[g][0]
            return featT[:, t * P:(t + 1) * P, first:first + len(GROUPS[g])]

        def z_source(stage, j, q):
            _, c0, c1 = STAGES[stage]
            rows = last_position(c1)
            view = gram_ps[stage % 2][QUAD * j:QUAD * j + rows, :].rearrange("i (k w) -> i k w", k=2)
            view = view[:, :, 0:SLOTS_PER_BANK * COLS].rearrange("i k (s g) -> i k s g", g=COLS)
            return view[:, :, :, 4 * c0 + q:rows:4].rearrange("i k s c -> i c k s")

        def z_target(stage, j, q):
            t, c0, c1 = STAGES[stage]
            rows = last_position(c1)
            c1 = c0 + len(range(4 * c0 + q, rows, 4))
            b0 = t * P + j * SLOTS
            return zT[QUAD * q:QUAD * q + rows, c0:c1, b0:b0 + SLOTS].rearrange("i c (k s) -> i c k s", k=2)

        def quadrants(stage):
            return range(copies(stage) // 2)

        def oh_ids_ps(k):
            return (h1_ps, h2_ps)[k % 2][0:RPARTS, :]

        @block.sync
        def _(sp):
            def load_table(k):
                if k >= 3:
                    sp.wait_ge(hi_ready, k - 2)
                    sp.wait_ge(lo_ready, k - 2)
                rows = tables[ONEHOT_TABLES[k]].rearrange("(p c) d -> p (c d)", c=RCHUNKS)
                sp.dma_start(table_sb[:, k % 3, :], rows).then_inc(table_in[k], 16)

            sp.dma_start(ids_sb[:, :], ids).then_inc(ids_in, 16)
            load_table(0)
            sp.dma_start(dense_sb[:, :, :], dense.rearrange("(t p) d -> p t d", p=P)).then_inc(dense_in, 16)
            for k in range(1, ONEHOTS):
                load_table(k)
            sp.dma_start(w_dense_sb[:, :, :], w_dense).then_inc(w_dense_in, 16)
            sp.dma_start(w_inter_sb[:, :, :], w_inter).then_inc(w_inter_in, 16)
            sp.dma_start(w2_sb[:, :, :], w2.rearrange("(k p) n -> p k n", p=P)).then_inc(w2_in, 16)
            sp.dma_start(w3_sb[:, :], w3).then_inc(small_in, 16)
            sp.dma_start(b1_sb[:, :], b1).then_inc(small_in, 16)
            sp.dma_start(b2_sb[:, :], b2).then_inc(small_in, 16)
            sp.wait_ge(y_ready, TILES)
            sp.dma_start(out.rearrange("b a -> a b"), y_sb[:, :]).then_inc(out_done, 16)
            sp.wait_ge(out_done, 16)

        @block.gpsimd
        def _(pool):
            pool.memset(ident[:, :], 0.0).then_inc(ident_zero, 1)
            pool.iota(rowno_i[:, :], pattern=[[1, RCHUNKS]], base=0, channel_multiplier=RCHUNKS) \
                .then_inc(rowno_int, 1)
            pool.wait_ge(ident_zero, 1)
            pool.affine_select(out=ident[:, :], in_=ident[:, :], compare_op=ALU.not_equal, fill=1.0,
                               base=0, pattern=[[-1, P]], channel_multiplier=1).then_inc(ident_ready, 1)
            pool.wait_ge(ids_in, 16)
            for t in range(TILES):
                for g, group in enumerate(GROUPS):
                    for pos in group:
                        table = FIELD_AT[pos] - 1
                        col = t * SPARSE + table
                        pool.indirect_dma_start(
                            out=gathered[:, t, pos - GATHERED[0], :], out_offset=None, in_=tables[table],
                            in_offset=bass.IndirectOffsetOnAxis(ap=ids_sb[:, col:col + 1], axis=0),
                        ).then_inc(rows_in[t][g], 16)

        @block.scalar
        def _(act):
            act.dma_start(oh_ids_sb[:, 0, :], oh_ids[0].partition_broadcast(RPARTS)).then_inc(oh_ids_in[0], 16)
            act.dma_start(oh_ids_sb[:, 1:, :], oh_ids[1:].partition_broadcast(RPARTS)).then_inc(oh_ids_in[1], 16)

            def onehot_to_featT(k):
                act.wait_ge(onehot_used, RCHUNKS * (k + 1))
                nc.scalar.activation(featT[:, :, 1 + k], fill_ps[(1 + k) % 2][:, :], ACT.Copy) \
                    .then_inc(fill_read[(1 + k) % 2], 1)

            def fill_to_featT(t, g):
                n = fill_no(t, g)
                if n % 2 == 1:
                    act.wait_ge(filled[1], transposed(n))
                    nc.scalar.activation(group_target(t, g), group_source(1, g), ACT.Copy) \
                        .then_inc(fill_read[1], 1)

            def products_to_zT(stage):
                act.wait_ge(gram_ready, stage + 1)
                for j in (2, 3):
                    for q in quadrants(stage):
                        nc.scalar.activation(z_target(stage, j, q), z_source(stage, j, q), ACT.Copy) \
                            .then_inc(z_act, 1)

            def hidden2(t):
                act.wait_ge(h2_psum, t + 1)
                for n in range(N2):
                    nc.scalar.activation(h2[:, n, :], h2_ps[:, n * P:(n + 1) * P], ACT.Relu,
                                         bias=b2_sb[:, n:n + 1]).then_inc(h2_ready, 1)

            act.wait_ge(rowno_ready, 2)
            for k in range(ONEHOTS):
                act.wait_ge(oh_ids_in[min(k, 1)], 16)
                if k >= 2:
                    act.wait_ge(onehot_dve, DVE_CHUNKS * (k - 1))
                nc.scalar.activation(oh_ids_ps(k), oh_ids_sb[:, k, :], ACT.Copy).then_inc(ids_psum, 1)
                act.wait_ge(table_in[k], 16)
                if k >= 2:
                    act.wait_ge(onehot_used, RCHUNKS * (k - 1))
                nc.scalar.activation(table_hi[:, k % 2, :], table_sb[:, k % 3, :], ACT.Copy).then_inc(hi_ready, 1)
                for c in range(DVE_CHUNKS, RCHUNKS):
                    done = k * (RCHUNKS - DVE_CHUNKS) + c - DVE_CHUNKS
                    if done:
                        act.wait_ge(onehot_act, done)
                    nc.scalar.activation(id_off[:, :], oh_ids_sb[:, k, :], ACT.Abs,
                                         bias=minus_rowno[:, c:c + 1]).then_inc(id_off_ready, 1)
                    if k > 0:
                        act.wait_ge(onehot_used, RCHUNKS * (k - 1) + c + 1)
                    act.wait_ge(id_off_ready, done + 1)
                    nc.scalar.activation(onehot[:, c, :], id_off[:, :], ACT.Relu, bias=1.0, scale=-1.0) \
                        .then_inc(onehot_act, 1)
                if k >= 1:
                    onehot_to_featT(k - 1)
            onehot_to_featT(ONEHOTS - 1)

            act.wait_ge(small_in, 48)
            act.wait_ge(zT_zeroed, 1)
            for stage, (t, c0, c1) in enumerate(STAGES):
                for g in groups_of_stage(stage):
                    fill_to_featT(t, g)
                    if t > 1 and g == L21_AFTER:
                        hidden2(t - 2)
                if stage == len(STAGES) - 2:
                    hidden2(LAST - 1)
                products_to_zT(stage)
            hidden2(LAST)

        @block.vector
        def _(dve):
            def fill_to_featT(t, g):
                n = fill_no(t, g)
                if n % 2 == 0:
                    dve.wait_ge(filled[0], transposed(n))
                    nc.vector.tensor_copy(group_target(t, g), group_source(0, g)).then_inc(fill_read[0], 1)

            def products_to_zT(stage):
                dve.wait_ge(gram_ready, stage + 1)
                for j in (0, 1):
                    for q in quadrants(stage):
                        nc.vector.tensor_copy(z_target(stage, j, q), z_source(stage, j, q)).then_inc(z_dve, 1)

            def hidden1(t):
                dve.wait_ge(h1_psum, t + 1)
                for n in range(N1):
                    nc.vector.tensor_scalar(h1[:, n, :], h1_ps[:, n * P:(n + 1) * P], b1_sb[:, n:n + 1], 0.0,
                                            ALU.add, ALU.max).then_inc(h1_ready, 1)

            def scores(t):
                dve.wait_ge(y_psum, t + 1)
                nc.vector.tensor_copy(y_sb[0:1, t * P:(t + 1) * P], h2_ps[0:1, N2 * P:(N2 + 1) * P]) \
                    .then_inc(y_ready, 1)

            nc.vector.memset(zT[:, :, :], 0.0).then_inc(zT_zeroed, 1)
            dve.wait_ge(rowno_int, 1)
            nc.vector.tensor_copy(rowno[:, :], rowno_i[:, :]).then_inc(rowno_ready, 1)
            nc.vector.tensor_scalar(minus_rowno[:, :], rowno_i[:, :], -1.0, None, ALU.mult).then_inc(rowno_ready, 1)
            dve.wait_ge(rowno_ready, 2)
            for k in range(ONEHOTS):
                dve.wait_ge(ids_psum, k + 1)
                for c in range(0, DVE_CHUNKS, DVE_STEP):
                    if k > 0:
                        dve.wait_ge(onehot_used, RCHUNKS * (k - 1) + c + DVE_STEP)
                    of_step = [RPARTS, DVE_STEP, BATCH]
                    nc.vector.tensor_tensor(onehot[:, c:c + DVE_STEP, :],
                                            oh_ids_ps(k).unsqueeze(1).to_broadcast(of_step),
                                            rowno[:, c:c + DVE_STEP].unsqueeze(2).to_broadcast(of_step),
                                            ALU.is_equal).then_inc(onehot_dve, DVE_STEP)
                    if c == 0:
                        dve.wait_ge(hi_ready, k + 1)
                        nc.vector.tensor_tensor(table_lo[:, k % 2, :], table_sb[:, k % 3, :],
                                                table_hi[:, k % 2, :].bitcast(fp32), ALU.subtract) \
                            .then_inc(lo_ready, 1)
                if k == 0:
                    dve.wait_ge(filled[0], 1)
                    nc.vector.tensor_copy(denseT[:, :], fill_ps[0][:, :])
                    nc.vector.tensor_copy(featT[:, :, 0], fill_ps[0][:, :]).then_inc(fill_read[0], 1)
            dve.wait_ge(w_dense_in, 16)
            nc.vector.tensor_tensor(w_dsum[:, :], w_dense_sb[:, 0, :], w_dense_sb[:, 1, :], ALU.add) \
                .then_inc(dsum_ready, 1)

            dve.wait_ge(small_in, 48)
            dve.wait_ge(zT_zeroed, 1)
            for stage, (t, c0, c1) in enumerate(STAGES):
                for g in groups_of_stage(stage):
                    fill_to_featT(t, g)
                    if t > 0 and g == L21_AFTER:
                        hidden1(t - 1)
                    if t > 1 and g == L3_AFTER:
                        scores(t - 2)
                if stage == len(STAGES) - 1:
                    scores(LAST - 1)
                products_to_zT(stage)
            hidden1(LAST)
            scores(LAST)

        @block.tensor
        def _(pe):
            def lookup(k):
                n = 1 + k
                if n >= 2:
                    pe.wait_ge(fill_read[n % 2], n // 2)
                pe.wait_ge(lo_ready, k + 1)
                pe.wait_ge(hi_ready, k + 1)
                for c in range(RCHUNKS):
                    rows = slice(c * DIM, (c + 1) * DIM)
                    if c < DVE_CHUNKS:
                        pe.wait_ge(onehot_dve, DVE_CHUNKS * k + c + 1)
                    else:
                        pe.wait_ge(onehot_act, (RCHUNKS - DVE_CHUNKS) * k + c + 1 - DVE_CHUNKS)
                    nc.tensor.matmul(fill_ps[n % 2][:, :], table_hi[:, k % 2, rows], onehot[:, c, :],
                                     start=(c == 0), stop=False)
                    last = nc.tensor.matmul(fill_ps[n % 2][:, :], table_lo[:, k % 2, rows], onehot[:, c, :],
                                            start=False, stop=(c == RCHUNKS - 1))
                    last.then_inc(onehot_used, 1)

            def fill(t, g):
                n = fill_no(t, g)
                pe.wait_ge(rows_in[t][g], 16 * len(GROUPS[g]))
                pe.wait_ge(fill_read[n % 2], n // 2)
                for i, pos in enumerate(GROUPS[g]):
                    last = nc.tensor.transpose(fill_ps[n % 2][:, i * P:(i + 1) * P],
                                               gathered[:, t, pos - GATHERED[0], :], ident[:, :])
                last.then_inc(filled[n % 2], 1)

            def fills_in_featT(upto):
                for bank in range(2):
                    pe.wait_ge(fill_read[bank], fills_of_bank(bank, upto))

            def gram(stage):
                t, c0, c1 = STAGES[stage]
                rows, first = last_position(c1), 4 * c0
                fills_in_featT(fill_no(t, groups_of_stage(stage)[-1]) + 1)
                if stage >= 2:
                    pe.wait_ge(z_dve, copies_done(stage - 2))
                    pe.wait_ge(z_act, copies_done(stage - 2))
                for s in range(SLOTS):
                    col = BANK * (s // SLOTS_PER_BANK) + COLS * (s % SLOTS_PER_BANK)
                    for j in range(4):
                        b = t * P + j * SLOTS + s
                        last = nc.tensor.matmul(
                            gram_ps[stage % 2][QUAD * j:QUAD * j + rows, col + first:col + rows],
                            featT[:, b, 0:rows], featT[:, b, 1 + first:1 + rows], start=True, stop=True)
                last.then_inc(gram_ready, 1)

            def layer1(stage):
                t, c0, c1 = STAGES[stage]
                tile = slice(t * P, (t + 1) * P)
                if stage == 0:
                    pe.wait_ge(dsum_ready, 1)
                    pe.wait_ge(w_inter_in, 16)
                pe.wait_ge(z_dve, copies_done(stage))
                pe.wait_ge(z_act, copies_done(stage))
                if t > 0 and c0 == 0:
                    pe.wait_ge(h1_ready, N1 * t)
                for n in range(N1):
                    units = slice(n * P, (n + 1) * P)
                    if c0 == 0:
                        nc.tensor.matmul(h1_ps[:, units], w_dsum[:, units], denseT[:, tile], start=(n == 0),
                                         stop=False, skip_group_check=True)
                    for c in range(c0, c1):
                        k = chunk_rows(c)
                        last = nc.tensor.matmul(h1_ps[:, units], w_inter_sb[0:k, c, units], zT[0:k, c, tile],
                                                start=False, stop=(c == CHUNKS - 1), skip_group_check=True)
                if c1 == CHUNKS:
                    last.then_inc(h1_psum, 1)

            def layer2(t):
                if t == 0:
                    pe.wait_ge(w2_in, 16)
                pe.wait_ge(h1_ready, N1 * (t + 1))
                if t > 0:
                    pe.wait_ge(y_ready, t)
                for n in range(N2):
                    for k in range(N1):
                        last = nc.tensor.matmul(h2_ps[:, n * P:(n + 1) * P], w2_sb[:, k, n * P:(n + 1) * P],
                                                h1[:, k, :], start=(k == 0), stop=(k == N1 - 1))
                last.then_inc(h2_psum, 1)

            def layer3(t):
                if t == 0:
                    pe.wait_ge(small_in, 48)
                pe.wait_ge(h2_ready, N2 * (t + 1))
                for k in range(N2):
                    last = nc.tensor.matmul(h2_ps[0:1, N2 * P:(N2 + 1) * P], w3_sb[:, k:k + 1], h2[:, k, :],
                                            start=(k == 0), stop=(k == N2 - 1))
                last.then_inc(y_psum, 1)

            pe.wait_ge(ident_ready, 1)
            pe.wait_ge(dense_in, 16)
            for t in range(TILES):
                last = nc.tensor.transpose(fill_ps[0][:, t * P:(t + 1) * P], dense_sb[:, t, :], ident[:, :])
            last.then_inc(filled[0], 1)
            for k in range(ONEHOTS):
                lookup(k)
            for stage, (t, c0, c1) in enumerate(STAGES):
                for g in groups_of_stage(stage):
                    fill(t, g)
                    if t > 1 and g == L21_AFTER:
                        layer2(t - 2)
                    if t > 0 and g == L21_AFTER:
                        layer1(stage - 1)
                    if t > 1 and g == L3_AFTER:
                        layer3(t - 2)
                if stage == len(STAGES) - 2:
                    layer2(LAST - 1)
                if stage == len(STAGES) - 1:
                    layer3(LAST - 1)
                if t == LAST and c0 > 0:
                    layer1(stage - 1)
                gram(stage)
            layer1(len(STAGES) - 1)
            layer2(LAST)
            layer3(LAST)


def first_layer_layout(w1):
    w = np.zeros((P, CHUNKS, HID1), w1.dtype)
    for g in range(1, FEATS):
        c, q = divmod(g - 1, 4)
        for i in range(g):
            lo, hi = sorted((FIELD_AT[i], FIELD_AT[g]))
            pair = lo * FEATS - lo * (lo + 1) // 2 + (hi - lo - 1)
            w[QUAD * q + i, c] = w1[DIM + pair]
    return w


def kernel(**inputs):
    import numpy as _np
    import concourse.bacc as _bacc
    from concourse import mybir as _mybir
    from concourse.bass_utils import run_bass_kernel_spmd as _run

    arr = {k: _np.ascontiguousarray(v) for k, v in inputs.items()}
    w1 = arr["W_top1"]
    data = {
        "dense": arr["r_dense_features"],
        "ids": _np.ascontiguousarray(arr["ids"].reshape(TILES, P, SPARSE).transpose(1, 0, 2).reshape(P, -1)),
        **{f"tbl_{n}": arr[f"tbl_{n}"] for n in range(SPARSE)},
        "oh_ids": _np.ascontiguousarray(arr["ids"][:, list(ONEHOT_TABLES)].T),
        "w_inter": first_layer_layout(w1),
        "w_dense": _np.ascontiguousarray(_np.stack([w1[:DIM], w1[-DIM:]], axis=1)),
        "b1": _np.ascontiguousarray(arr["b_top1"].reshape(N1, P).T),
        "w2": arr["W_top2"],
        "b2": _np.ascontiguousarray(arr["b_top2"].reshape(N2, P).T),
        "w3": _np.ascontiguousarray(arr["W_top3"].reshape(N2, P).T),
    }
    nc = _bacc.Bacc("TRN2", target_bir_lowering=False, num_devices=1)
    ap = {k: nc.dram_tensor(k, v.shape, _mybir.dt.from_np(v.dtype), kind="ExternalInput").ap()
          for k, v in data.items()}
    out = nc.dram_tensor("scores", (BATCH, 1), _mybir.dt.float32, kind="ExternalOutput").ap()
    tower(nc, ap["dense"], ap["ids"], ap["oh_ids"], [ap[f"tbl_{n}"] for n in range(SPARSE)], ap["w_inter"], ap["w_dense"],
          ap["b1"], ap["w2"], ap["b2"], ap["w3"], out)
    r = _run(nc, [data], core_ids=[0])
    return r.results[0]["scores"]
```

```python
from contextlib import ExitStack

import numpy as np

import concourse.bass as bass
from concourse import mybir

P = 128
QUAD = 32
BATCH, DIM, SPARSE = 512, 128, 26
FEATS = SPARSE + 1
TILES = BATCH // P
SLOTS = P // 4
HID1, HID2 = 512, 256
N1, N2 = HID1 // P, HID2 // P
COLS = FEATS - 1
CHUNKS = -(-COLS // 4)
BANK = 512
SLOTS_PER_BANK = 16

ONEHOT_TABLES = (0, 1, 3, 6, 8)
ONEHOTS = len(ONEHOT_TABLES)
ROWS = 1000
RCHUNKS = 8
RPARTS = ROWS // RCHUNKS
DVE_CHUNKS = 6
DVE_STEP = 3
FIELD_AT = [0] + [1 + n for n in ONEHOT_TABLES] + [1 + n for n in range(SPARSE) if n not in ONEHOT_TABLES]
GATHERED = list(range(1 + ONEHOTS, FEATS))
GROUPS = [[g for g in range(4 * c + 1, 4 * c + 5) if g in GATHERED] for c in range(CHUNKS)]
GROUPS = [group for group in GROUPS if group]
LAST = TILES - 1
LAST_CUT = 5
STAGES = [(t, 0, CHUNKS) for t in range(LAST)] + [(LAST, 0, LAST_CUT), (LAST, LAST_CUT, CHUNKS)]
BESIDE = (3, 0, 0, 2)

AFTER_LOOKUP = [(), (0, 1), (2,), (3,), ()]

L1_AFTER, L3_AFTER = 1, 3


def last_position(c1):
    return min(4 * c1, COLS)


def copies(stage):
    _, c0, c1 = STAGES[stage]
    return 2 * min(4, last_position(c1) - 4 * c0)


def copies_done(stage):
    return sum(copies(u) for u in range(stage + 1))


def groups_of_stage(stage):
    t, c0, c1 = STAGES[stage]
    return [g for g, group in enumerate(GROUPS) if 4 * c0 < group[-1] <= last_position(c1)]


def chunk_rows(c):
    return QUAD * (min(4, COLS - 4 * c) - 1) + FEATS - 1


def tower(nc, dense, ids, oh_ids, tables, w_inter, w_dense, b1, w2, b2, w3, out):
    fp32, fp32r, i32 = mybir.dt.float32, mybir.dt.float32r, mybir.dt.int32
    ALU, ACT = mybir.AluOpType, mybir.ActivationFunctionType

    with ExitStack() as ctx:
        def sb(name, shape, dt=fp32):
            return ctx.enter_context(nc.sbuf_tensor(name, shape, dt))

        def pb(name, cols):
            return ctx.enter_context(nc.psum_tensor(name, [P, cols], fp32))

        def sem(name):
            return ctx.enter_context(nc.semaphore(name))

        ids_sb = sb("ids_sb", [P, TILES * SPARSE], i32)
        oh_ids_rows = sb("oh_ids_rows", [ONEHOTS, BATCH], i32)
        oh_ids_r = sb("oh_ids_r", [ONEHOTS, BATCH], fp32r)
        row_pick = sb("row_pick", [ONEHOTS, ONEHOTS, RPARTS], fp32r)
        oh_ids_sb = sb("oh_ids_sb", [RPARTS, ONEHOTS, BATCH], i32)
        rowno_i = sb("rowno_i", [RPARTS, RCHUNKS], i32)
        rowno = sb("rowno", [RPARTS, RCHUNKS])
        minus_rowno = sb("minus_rowno", [RPARTS, RCHUNKS])
        id_off = sb("id_off", [RPARTS, BATCH])
        table_sb = sb("table_sb", [RPARTS, 3, RCHUNKS * DIM])
        table_hi = sb("table_hi", [RPARTS, 2, RCHUNKS * DIM], fp32r)
        table_lo = sb("table_lo", [RPARTS, 2, RCHUNKS * DIM], fp32r)
        onehot = sb("onehot", [RPARTS, RCHUNKS, BATCH], fp32r)
        dense_sb = sb("dense_sb", [P, TILES, DIM])
        gathered = sb("gathered", [P, TILES, len(GATHERED), DIM])
        featT = sb("featT", [P, BATCH, FEATS])
        zT = sb("zT", [P, CHUNKS, BATCH])
        w_inter_sb = sb("w_inter_sb", [P, CHUNKS, HID1])
        w_dense_sb = sb("w_dense_sb", [P, 2, HID1])
        w_dsum = sb("w_dsum", [P, HID1])
        w2_sb = sb("w2_sb", [P, N1, HID2])
        w3_sb = sb("w3_sb", [P, N2])
        b1_sb = sb("b1_sb", [P, N1])
        b2_sb = sb("b2_sb", [P, N2])
        h1 = sb("h1", [P, N1, P])
        h2 = sb("h2", [P, N2, P])
        y_sb = sb("y_sb", [1, BATCH])
        ident = sb("ident", [P, P])

        fill_ps = [pb(f"fill_ps{i}", BANK) for i in range(2)]
        gram_ps = [pb(f"gram_ps{i}", 2 * BANK) for i in range(2)]
        h1_ps = pb("h1_ps", BANK)
        h2_ps = pb("h2_ps", BANK)

        ids_in = sem("ids_in")
        dense_in = sem("dense_in")
        table_in = [sem(f"table_in{k}") for k in range(ONEHOTS)]
        oh_ids_in = [sem(f"oh_ids_in{i}") for i in range(2)]
        oh_rows_in = sem("oh_rows_in")
        oh_rows_ready = sem("oh_rows_ready")
        row_pick_ready = sem("row_pick_ready")
        rowno_int = sem("rowno_int")
        minus_ready = sem("minus_ready")
        rowno_ready = sem("rowno_ready")
        hi_ready = sem("hi_ready")
        lo_ready = sem("lo_ready")
        ids_psum = sem("ids_psum")
        onehot_dve = sem("onehot_dve")
        onehot_act = sem("onehot_act")
        id_off_ready = sem("id_off_ready")
        onehot_used = sem("onehot_used")
        lookup_read = sem("lookup_read")
        w_inter_in = sem("w_inter_in")
        w_dense_in = sem("w_dense_in")
        w2_in = sem("w2_in")
        small_in = sem("small_in")
        rows_in = [[sem(f"rows_in{t}_{g}") for g in range(len(GROUPS))] for t in range(TILES)]
        ident_zero = sem("ident_zero")
        ident_ready = sem("ident_ready")
        zT_zeroed = sem("zT_zeroed")
        dsum_ready = sem("dsum_ready")
        filled = [sem(f"filled{i}") for i in range(2)]
        fill_read = [sem(f"fill_read{i}") for i in range(2)]
        gram_ready = sem("gram_ready")
        z_dve = sem("z_dve")
        z_act = sem("z_act")
        h1_psum = sem("h1_psum")
        h1_ready = sem("h1_ready")
        h1_act = sem("h1_act")
        h2_psum = sem("h2_psum")
        h2_ready = sem("h2_ready")
        y_psum = sem("y_psum")
        y_ready = sem("y_ready")
        out_done = sem("out_done")

        block = ctx.enter_context(nc.Block())

        def fill_no(t, g):
            return 1 + t * len(GROUPS) + g

        def dve_reads(t, g):
            return fill_no(t, g) % 2 == 0 and not transposed_early(t, g)

        def fills_of_bank(bank, upto):
            return (upto - bank + 1) // 2

        def transposed(n):
            return n // 2 + 1

        def lookup_ps(k):
            return gram_ps[k % 2][:, 0:BATCH]

        def group_source(bank, g):
            n = len(GROUPS[g])
            return fill_ps[bank][:, 0:n * P].rearrange("d (f b) -> d b f", f=n)

        def group_target(t, g):
            first = GROUPS[g][0]
            return featT[:, t * P:(t + 1) * P, first:first + len(GROUPS[g])]

        def z_source(stage, j, q):
            _, c0, c1 = STAGES[stage]
            rows = last_position(c1)
            view = gram_ps[stage % 2][QUAD * j:QUAD * j + rows, :].rearrange("i (k w) -> i k w", k=2)
            view = view[:, :, 0:SLOTS_PER_BANK * COLS].rearrange("i k (s g) -> i k s g", g=COLS)
            return view[:, :, :, 4 * c0 + q:rows:4].rearrange("i k s c -> i c k s")

        def z_target(stage, j, q):
            t, c0, c1 = STAGES[stage]
            rows = last_position(c1)
            c1 = c0 + len(range(4 * c0 + q, rows, 4))
            b0 = t * P + j * SLOTS
            return zT[QUAD * q:QUAD * q + rows, c0:c1, b0:b0 + SLOTS].rearrange("i c (k s) -> i c k s", k=2)

        def transposed_early(t, g):
            return t == 0 and any(g in groups for groups in AFTER_LOOKUP)

        def quadrants(stage):
            return range(copies(stage) // 2)

        def layer1_ps(t, n):
            if t == LAST and n >= N1 // 2:
                return gram_ps[(len(STAGES) - 2) % 2][:, (n - N1 // 2) * P:(n - N1 // 2 + 1) * P]
            return h1_ps[:, n * P:(n + 1) * P]

        def oh_ids_ps(k):
            return (h1_ps, h2_ps)[k % 2][0:RPARTS, :]

        @block.sync
        def _(sp):
            def load_table(k):
                if k >= 3:
                    sp.wait_ge(hi_ready, k - 2)
                    sp.wait_ge(lo_ready, k - 2)
                rows = tables[ONEHOT_TABLES[k]].rearrange("(p c) d -> p (c d)", c=RCHUNKS)
                sp.dma_start(table_sb[:, k % 3, :], rows).then_inc(table_in[k], 16)

            sp.dma_start(ids_sb[:, :], ids).then_inc(ids_in, 16)
            load_table(0)
            sp.dma_start(oh_ids_sb[:, 0, :], oh_ids[0].partition_broadcast(RPARTS)).then_inc(oh_ids_in[0], 16)
            load_table(1)
            sp.dma_start(oh_ids_sb[:, 1:, :], oh_ids[1:].partition_broadcast(RPARTS)).then_inc(oh_ids_in[1], 16)
            sp.dma_start(dense_sb[:, :, :], dense.rearrange("(t p) d -> p t d", p=P)).then_inc(dense_in, 16)
            for k in range(2, ONEHOTS):
                load_table(k)
            sp.dma_start(w_dense_sb[:, :, :], w_dense).then_inc(w_dense_in, 16)
            sp.dma_start(w_inter_sb[:, :, :], w_inter).then_inc(w_inter_in, 16)
            sp.dma_start(w2_sb[:, :, :], w2.rearrange("(k p) n -> p k n", p=P)).then_inc(w2_in, 16)
            sp.dma_start(w3_sb[:, :], w3).then_inc(small_in, 16)
            sp.dma_start(b1_sb[:, :], b1).then_inc(small_in, 16)
            sp.dma_start(b2_sb[:, :], b2).then_inc(small_in, 16)
            sp.wait_ge(y_ready, TILES)
            sp.dma_start(out.rearrange("b a -> a b"), y_sb[:, :]).then_inc(out_done, 16)
            sp.wait_ge(out_done, 16)

        @block.gpsimd
        def _(pool):
            pool.memset(ident[:, :], 0.0).then_inc(ident_zero, 1)
            pool.iota(rowno_i[:, :], pattern=[[1, RCHUNKS]], base=0, channel_multiplier=RCHUNKS) \
                .then_inc(rowno_int, 1)
            pool.wait_ge(ident_zero, 1)
            pool.affine_select(out=ident[:, :], in_=ident[:, :], compare_op=ALU.not_equal, fill=1.0,
                               base=0, pattern=[[-1, P]], channel_multiplier=1).then_inc(ident_ready, 1)
            pool.wait_ge(ids_in, 16)
            for t in range(TILES):
                for g, group in enumerate(GROUPS):
                    for pos in group:
                        table = FIELD_AT[pos] - 1
                        col = t * SPARSE + table
                        pool.indirect_dma_start(
                            out=gathered[:, t, pos - GATHERED[0], :], out_offset=None, in_=tables[table],
                            in_offset=bass.IndirectOffsetOnAxis(ap=ids_sb[:, col:col + 1], axis=0),
                        ).then_inc(rows_in[t][g], 16)

        @block.scalar
        def _(act):
            act.dma_start(oh_ids_rows[:, :], oh_ids).then_inc(oh_rows_in, 16)

            def onehot_to_featT(k):
                act.wait_ge(onehot_used, RCHUNKS * (k + 1))
                nc.scalar.activation(featT[:, :, 1 + k], lookup_ps(k), ACT.Copy).then_inc(lookup_read, 1)

            def fill_to_featT(t, g):
                n = fill_no(t, g)
                if not dve_reads(t, g):
                    act.wait_ge(filled[n % 2], transposed(n))
                    nc.scalar.activation(group_target(t, g), group_source(n % 2, g), ACT.Copy) \
                        .then_inc(fill_read[n % 2], 1)

            def products_to_zT(stage):
                act.wait_ge(gram_ready, stage + 1)
                for j in (2, 3):
                    for q in quadrants(stage):
                        nc.scalar.activation(z_target(stage, j, q), z_source(stage, j, q), ACT.Copy) \
                            .then_inc(z_act, 1)

            def hidden1_last_half():
                act.wait_ge(h1_psum, LAST + 2)
                for n in range(N1 // 2, N1):
                    nc.scalar.activation(h1[:, n, :], layer1_ps(LAST, n), ACT.Relu, bias=b1_sb[:, n:n + 1]) \
                        .then_inc(h1_act, 1)

            def hidden2(t):
                act.wait_ge(h2_psum, t + 1)
                for n in range(N2):
                    nc.scalar.activation(h2[:, n, :], h2_ps[:, n * P:(n + 1) * P], ACT.Relu,
                                         bias=b2_sb[:, n:n + 1]).then_inc(h2_ready, 1)

            def high_parts(k):
                act.wait_ge(table_in[k], 16)
                if k >= 2:
                    act.wait_ge(onehot_used, RCHUNKS * (k - 1))
                nc.scalar.activation(table_hi[:, k % 2, :], table_sb[:, k % 3, :], ACT.Copy).then_inc(hi_ready, 1)

            act.wait_ge(rowno_int, 1)
            nc.scalar.activation(minus_rowno[:, :], rowno_i[:, :], ACT.Copy, scale=-1.0).then_inc(minus_ready, 1)
            act.wait_ge(oh_rows_in, 16)
            nc.scalar.activation(oh_ids_r[:, :], oh_ids_rows[:, :], ACT.Copy).then_inc(oh_rows_ready, 1)
            high_parts(0)
            act.wait_ge(minus_ready, 1)
            for k in range(ONEHOTS):
                act.wait_ge(oh_ids_in[min(k, 1)], 16)
                for c in range(DVE_CHUNKS, RCHUNKS):
                    done = k * (RCHUNKS - DVE_CHUNKS) + c - DVE_CHUNKS
                    if done:
                        act.wait_ge(onehot_act, done)
                    nc.scalar.activation(id_off[:, :], oh_ids_sb[:, k, :], ACT.Abs,
                                         bias=minus_rowno[:, c:c + 1]).then_inc(id_off_ready, 1)
                    if k > 0:
                        act.wait_ge(onehot_used, RCHUNKS * (k - 1) + c + 1)
                    act.wait_ge(id_off_ready, done + 1)
                    nc.scalar.activation(onehot[:, c, :], id_off[:, :], ACT.Relu, bias=1.0, scale=-1.0) \
                        .then_inc(onehot_act, 1)
                if k + 1 < ONEHOTS:
                    high_parts(k + 1)
                if k == 1:
                    act.wait_ge(filled[0], 1)
                    nc.scalar.activation(featT[:, :, 0], fill_ps[0][:, :], ACT.Copy).then_inc(fill_read[0], 1)
                if k >= 1:
                    onehot_to_featT(k - 1)
                    for g in AFTER_LOOKUP[k - 1]:
                        fill_to_featT(0, g)
            onehot_to_featT(ONEHOTS - 1)
            for g in AFTER_LOOKUP[ONEHOTS - 1]:
                fill_to_featT(0, g)

            act.wait_ge(small_in, 48)
            act.wait_ge(zT_zeroed, 2)
            for stage, (t, c0, c1) in enumerate(STAGES):
                for g in groups_of_stage(stage):
                    if not transposed_early(t, g):
                        fill_to_featT(t, g)
                products_to_zT(stage)
                if t > 0 and c0 == 0:
                    hidden2(t - 1)
            hidden1_last_half()
            hidden2(LAST)

        @block.vector
        def _(dve):
            def fill_to_featT(t, g):
                n = fill_no(t, g)
                if dve_reads(t, g):
                    dve.wait_ge(filled[0], transposed(n))
                    nc.vector.tensor_copy(group_target(t, g), group_source(0, g)).then_inc(fill_read[0], 1)

            def products_to_zT(stage):
                dve.wait_ge(gram_ready, stage + 1)
                for j in (0, 1):
                    for q in quadrants(stage):
                        nc.vector.tensor_copy(z_target(stage, j, q), z_source(stage, j, q)).then_inc(z_dve, 1)

            def hidden1(t):
                dve.wait_ge(h1_psum, t + 1)
                for n in range(N1 // 2 if t == LAST else N1):
                    nc.vector.tensor_scalar(h1[:, n, :], layer1_ps(t, n), b1_sb[:, n:n + 1], 0.0,
                                            ALU.add, ALU.max).then_inc(h1_ready, 1)

            def scores(t):
                dve.wait_ge(y_psum, t + 1)
                nc.vector.tensor_copy(y_sb[0:1, t * P:(t + 1) * P], h2_ps[0:1, N2 * P:(N2 + 1) * P]) \
                    .then_inc(y_ready, 1)

            nc.vector.memset(zT[:, :, 0:LAST * P], 0.0).then_inc(zT_zeroed, 1)
            dve.wait_ge(ident_ready, 1)
            of_pick = [ONEHOTS, ONEHOTS, RPARTS]
            nc.vector.tensor_copy(row_pick[:, :, :], ident[0:ONEHOTS, 0:ONEHOTS].unsqueeze(2).to_broadcast(of_pick)) \
                .then_inc(row_pick_ready, 1)
            dve.wait_ge(rowno_int, 1)
            nc.vector.tensor_copy(rowno[:, :], rowno_i[:, :]).then_inc(rowno_ready, 1)
            dve.wait_ge(rowno_ready, 1)
            for k in range(ONEHOTS):
                dve.wait_ge(ids_psum, k + 1)
                for c in range(0, DVE_CHUNKS, DVE_STEP):
                    if k > 0:
                        dve.wait_ge(onehot_used, RCHUNKS * (k - 1) + c + DVE_STEP)
                    of_step = [RPARTS, DVE_STEP, BATCH]
                    nc.vector.tensor_tensor(onehot[:, c:c + DVE_STEP, :],
                                            oh_ids_ps(k).unsqueeze(1).to_broadcast(of_step),
                                            rowno[:, c:c + DVE_STEP].unsqueeze(2).to_broadcast(of_step),
                                            ALU.is_equal).then_inc(onehot_dve, DVE_STEP)
                    if c == 0:
                        dve.wait_ge(hi_ready, k + 1)
                        nc.vector.tensor_tensor(table_lo[:, k % 2, :], table_sb[:, k % 3, :],
                                                table_hi[:, k % 2, :].bitcast(fp32), ALU.subtract) \
                            .then_inc(lo_ready, 1)
            nc.vector.memset(zT[:, :, LAST * P:], 0.0).then_inc(zT_zeroed, 1)
            dve.wait_ge(w_dense_in, 16)
            nc.vector.tensor_tensor(w_dsum[:, :], w_dense_sb[:, 0, :], w_dense_sb[:, 1, :], ALU.add) \
                .then_inc(dsum_ready, 1)

            dve.wait_ge(small_in, 48)
            dve.wait_ge(zT_zeroed, 2)
            for stage, (t, c0, c1) in enumerate(STAGES):
                for g in groups_of_stage(stage):
                    if not transposed_early(t, g):
                        fill_to_featT(t, g)
                    if t > 1 and g == L3_AFTER:
                        scores(t - 2)
                if t > 0 and c0 == 0:
                    hidden1(t - 1)
                products_to_zT(stage)
            scores(LAST - 1)
            hidden1(LAST)
            scores(LAST)

        @block.tensor
        def _(pe):
            def lookup(k):
                if k >= 2:
                    pe.wait_ge(lookup_read, k - 1)
                pe.wait_ge(lo_ready, k + 1)
                pe.wait_ge(hi_ready, k + 1)
                for c in range(RCHUNKS):
                    rows = slice(c * DIM, (c + 1) * DIM)
                    if c < DVE_CHUNKS:
                        pe.wait_ge(onehot_dve, DVE_CHUNKS * k + c + 1)
                    else:
                        pe.wait_ge(onehot_act, (RCHUNKS - DVE_CHUNKS) * k + c + 1 - DVE_CHUNKS)
                    nc.tensor.matmul(lookup_ps(k), table_hi[:, k % 2, rows], onehot[:, c, :],
                                     start=(c == 0), stop=False)
                    last = nc.tensor.matmul(lookup_ps(k), table_lo[:, k % 2, rows], onehot[:, c, :],
                                            start=False, stop=(c == RCHUNKS - 1))
                    last.then_inc(onehot_used, 1)

            def spread_ids(k):
                if k == 0:
                    pe.wait_ge(row_pick_ready, 1)
                    pe.wait_ge(oh_rows_ready, 1)
                if k >= 2:
                    pe.wait_ge(onehot_dve, DVE_CHUNKS * (k - 1))
                nc.tensor.matmul(oh_ids_ps(k), row_pick[:, k, :], oh_ids_r[:, :], start=True, stop=True) \
                    .then_inc(ids_psum, 1)

            def fill(t, g):
                n = fill_no(t, g)
                pe.wait_ge(rows_in[t][g], 16 * len(GROUPS[g]))
                if n >= 2:
                    pe.wait_ge(fill_read[n % 2], n // 2)
                for i, pos in enumerate(GROUPS[g]):
                    last = nc.tensor.transpose(fill_ps[n % 2][:, i * P:(i + 1) * P],
                                               gathered[:, t, pos - GATHERED[0], :], ident[:, :])
                last.then_inc(filled[n % 2], 1)

            def fills_in_featT(upto):
                for bank in range(2):
                    pe.wait_ge(fill_read[bank], fills_of_bank(bank, upto))

            def products_start(stage):
                t, c0, c1 = STAGES[stage]
                fills_in_featT(fill_no(t, groups_of_stage(stage)[-1]) + 1)
                if stage == 0:
                    pe.wait_ge(lookup_read, ONEHOTS)
                if stage >= 2:
                    pe.wait_ge(z_dve, copies_done(stage - 2))
                    pe.wait_ge(z_act, copies_done(stage - 2))

            def products(stage, part):
                t, c0, c1 = STAGES[stage]
                rows, first = last_position(c1), 4 * c0
                for s in range(part * SLOTS // N1, (part + 1) * SLOTS // N1):
                    col = BANK * (s // SLOTS_PER_BANK) + COLS * (s % SLOTS_PER_BANK)
                    for j in range(4):
                        b = t * P + j * SLOTS + s
                        last = nc.tensor.matmul(
                            gram_ps[stage % 2][QUAD * j:QUAD * j + rows, col + first:col + rows],
                            featT[:, b, 0:rows], featT[:, b, 1 + first:1 + rows], start=True, stop=True)
                if part == N1 - 1:
                    last.then_inc(gram_ready, 1)

            def layer1_start(stage):
                t, c0, c1 = STAGES[stage]
                if stage == 0:
                    pe.wait_ge(dsum_ready, 1)
                    pe.wait_ge(w_inter_in, 16)
                pe.wait_ge(z_dve, copies_done(stage))
                pe.wait_ge(z_act, copies_done(stage))
                if t > 0 and c0 == 0:
                    pe.wait_ge(h1_ready, N1 * t)

            def layer1(stage, n):
                t, c0, c1 = STAGES[stage]
                tile = slice(t * P, (t + 1) * P)
                units = slice(n * P, (n + 1) * P)
                if c0 == 0:
                    nc.tensor.matmul(layer1_ps(t, n), w_dsum[:, units], featT[:, tile, 0],
                                     start=(n == 0 or (t == LAST and n == N1 // 2)),
                                     stop=False, skip_group_check=True)
                for c in range(c0, c1):
                    k = chunk_rows(c)
                    last = nc.tensor.matmul(layer1_ps(t, n), w_inter_sb[0:k, c, units], zT[0:k, c, tile],
                                            start=False, stop=(c == CHUNKS - 1), skip_group_check=True)
                if c1 == CHUNKS and (n == N1 - 1 or (t == LAST and n == N1 // 2 - 1)):
                    last.then_inc(h1_psum, 1)

            def layer1_before(stage):
                layer1_start(stage)
                for n in range(N1 - BESIDE[stage]):
                    layer1(stage, n)

            def layer2(t):
                if t == 0:
                    pe.wait_ge(w2_in, 16)
                else:
                    pe.wait_ge(y_ready, t)
                for half in range(2):
                    if half == 0 or t < LAST:
                        pe.wait_ge(h1_ready, N1 * t + (half + 1) * N1 // 2)
                    else:
                        pe.wait_ge(h1_act, N1 // 2)
                    for n in range(N2):
                        for k in range(half * N1 // 2, (half + 1) * N1 // 2):
                            last = nc.tensor.matmul(h2_ps[:, n * P:(n + 1) * P], w2_sb[:, k, n * P:(n + 1) * P],
                                                    h1[:, k, :], start=(n == 0 and k == 0), stop=(k == N1 - 1),
                                                    skip_group_check=True)
                last.then_inc(h2_psum, 1)

            def layer3(t):
                if t == 0:
                    pe.wait_ge(small_in, 48)
                pe.wait_ge(h2_ready, N2 * (t + 1))
                for k in range(N2):
                    last = nc.tensor.matmul(h2_ps[0:1, N2 * P:(N2 + 1) * P], w3_sb[:, k:k + 1], h2[:, k, :],
                                            start=(k == 0), stop=(k == N2 - 1))
                last.then_inc(y_psum, 1)

            spread_ids(0)
            for k in range(ONEHOTS):
                if k + 1 < ONEHOTS:
                    spread_ids(k + 1)
                lookup(k)
                if k == 0:
                    pe.wait_ge(ident_ready, 1)
                    pe.wait_ge(dense_in, 16)
                    for t in range(TILES):
                        last = nc.tensor.transpose(fill_ps[0][:, t * P:(t + 1) * P], dense_sb[:, t, :], ident[:, :])
                    last.then_inc(filled[0], 1)
                for g in AFTER_LOOKUP[k]:
                    fill(0, g)
            for stage, (t, c0, c1) in enumerate(STAGES):
                for g in groups_of_stage(stage):
                    if not transposed_early(t, g):
                        fill(t, g)
                    if t > 0 and g == L1_AFTER:
                        layer1_before(stage - 1)
                    if t > 1 and g == L3_AFTER:
                        layer3(t - 2)
                if t == LAST and c0 > 0:
                    layer1_before(stage - 1)
                products_start(stage)
                for part in range(N1):
                    if stage > 0 and part >= N1 - BESIDE[stage - 1]:
                        layer1(stage - 1, part)
                    products(stage, part)
                if t > 0 and c0 == 0:
                    layer2(t - 1)
            layer3(LAST - 1)
            layer1_start(len(STAGES) - 1)
            for n in range(N1):
                layer1(len(STAGES) - 1, n)
            layer2(LAST)
            layer3(LAST)


def first_layer_layout(w1):
    w = np.zeros((P, CHUNKS, HID1), w1.dtype)
    for g in range(1, FEATS):
        c, q = divmod(g - 1, 4)
        for i in range(g):
            lo, hi = sorted((FIELD_AT[i], FIELD_AT[g]))
            pair = lo * FEATS - lo * (lo + 1) // 2 + (hi - lo - 1)
            w[QUAD * q + i, c] = w1[DIM + pair]
    return w


def kernel(**inputs):
    import numpy as _np
    import concourse.bacc as _bacc
    from concourse import mybir as _mybir
    from concourse.bass_utils import run_bass_kernel_spmd as _run

    arr = {k: _np.ascontiguousarray(v) for k, v in inputs.items()}
    w1 = arr["W_top1"]
    data = {
        "dense": arr["r_dense_features"],
        "ids": _np.ascontiguousarray(arr["ids"].reshape(TILES, P, SPARSE).transpose(1, 0, 2).reshape(P, -1)),
        **{f"tbl_{n}": arr[f"tbl_{n}"] for n in range(SPARSE)},
        "oh_ids": _np.ascontiguousarray(arr["ids"][:, list(ONEHOT_TABLES)].T),
        "w_inter": first_layer_layout(w1),
        "w_dense": _np.ascontiguousarray(_np.stack([w1[:DIM], w1[-DIM:]], axis=1)),
        "b1": _np.ascontiguousarray(arr["b_top1"].reshape(N1, P).T),
        "w2": arr["W_top2"],
        "b2": _np.ascontiguousarray(arr["b_top2"].reshape(N2, P).T),
        "w3": _np.ascontiguousarray(arr["W_top3"].reshape(N2, P).T),
    }
    nc = _bacc.Bacc("TRN2", target_bir_lowering=False, num_devices=1)
    ap = {k: nc.dram_tensor(k, v.shape, _mybir.dt.from_np(v.dtype), kind="ExternalInput").ap()
          for k, v in data.items()}
    out = nc.dram_tensor("scores", (BATCH, 1), _mybir.dt.float32, kind="ExternalOutput").ap()
    tower(nc, ap["dense"], ap["ids"], ap["oh_ids"], [ap[f"tbl_{n}"] for n in range(SPARSE)], ap["w_inter"], ap["w_dense"],
          ap["b1"], ap["w2"], ap["b2"], ap["w3"], out)
    r = _run(nc, [data], core_ids=[0])
    return r.results[0]["scores"]
```
